# Optimizing a Trainium2 kernel written in Bass

```python
import numpy as np
import jax
import jax.numpy as jnp

def _softmax(x, axis=-1):
    return jax.nn.softmax(x, axis=axis)

def _gelu(x):
    return jax.nn.gelu(x, approximate=True)

def _silu(x):
    return jax.nn.silu(x)

def _sigmoid(x):
    return jax.nn.sigmoid(x)

def _layernorm(x, axis=-1, eps=1e-05):
    m = jnp.mean(x, axis=axis, keepdims=True)
    v = jnp.var(x, axis=axis, keepdims=True)
    return (x - m) / jnp.sqrt(v + eps)

def _scatter_add(tgt, idx, src, axis=0):
    return tgt.at[idx].add(src)

def _segment_sum(src, seg, n):
    return jax.ops.segment_sum(src, seg, n)
kernel_name = 'mk_xattn_seq_d1_seqx_r8_1ea554'

def setup_inputs(seed: int=0):
    np.random.seed(seed)
    _w = jnp.asarray

    def _rec_inputs():
        import jax
        import jax.numpy as jnp
        _rk = jax.random.key(seed)
        x = -0.000125 + 0.9999 * jax.random.normal(jax.random.fold_in(_rk, 1), (32, 56, 512), jnp.float32)
        _lenS = 56 - jax.random.randint(jax.random.fold_in(_rk, 7), (32,), 0, max(1, 56 // 4) + 1, jnp.int32)
        _lenS2 = 1500 - jax.random.randint(jax.random.fold_in(_rk, 8), (32,), 0, max(1, 1500 // 4) + 1, jnp.int32)
        _ctx_4096P = jax.random.normal(jax.random.fold_in(_rk, 11), (32, 16, 512), jnp.float32)
        _ctx_4096c = jax.random.dirichlet(jax.random.fold_in(_rk, 511), 0.3 * jnp.ones((16,), jnp.float32), (32, 1500))
        _ctx_4096t = jnp.einsum('bsk,bkd->bsd', _ctx_4096c, _ctx_4096P)
        _ctx_4096t = _ctx_4096t * jax.lax.rsqrt(jnp.mean(jnp.square(_ctx_4096t)) + 1e-12) * 0.953939
        ctx_4096 = 0.000227908 + 0.99994 * (_ctx_4096t + 0.3 * jax.random.normal(jax.random.fold_in(_rk, 611), (32, 1500, 512), jnp.float32))
        _validS = jnp.arange(56)[None, :] < _lenS[:, None]
        _validS2 = jnp.arange(1500)[None, :] < _lenS2[:, None]
        _causal = jnp.tril(jnp.ones((56, 56), dtype=bool))
        mask_BxS2_bf1 = jnp.ones((32, 1500), dtype=bool)
        return (x, ctx_4096, mask_BxS2_bf1)
    x, ctx_4096, mask_BxS2_bf1 = _rec_inputs()

    def _L0_xattn_setup():
        import jax, jax.numpy as jnp
        import numpy as np
        HIDDEN = 512
        HEADS = 32
        HEAD_DIM = HIDDEN // HEADS
        LN_EPS = 1e-05

        def _split_heads(x):
            B, S, _ = x.shape
            return x.reshape(B, S, HEADS, HEAD_DIM).transpose(0, 2, 1, 3)
        key = jax.random.key(seed)
        ks = jax.random.split(key, 7)
        B, S, SLOTS = (2, 512, 128)
        hidden_states = jax.random.normal(ks[0], (B, S, HIDDEN), dtype=jnp.float32)
        memory_keys = jax.random.normal(ks[1], (B, SLOTS, HIDDEN), dtype=jnp.float32)
        memory_values = jax.random.normal(ks[2], (B, SLOTS, HIDDEN), dtype=jnp.float32)
        attention_mask = jnp.ones((B, SLOTS), dtype=jnp.bool_)
        Wq = jax.random.normal(ks[3], (HIDDEN, HIDDEN), dtype=jnp.float32) / np.sqrt(HIDDEN)
        Wout = jax.random.normal(ks[4], (HIDDEN, HIDDEN), dtype=jnp.float32) / np.sqrt(HIDDEN)
        ln_gamma = jnp.ones((HIDDEN,), dtype=jnp.float32)
        ln_beta = jnp.zeros((HIDDEN,), dtype=jnp.float32)
        return dict(hidden_states=hidden_states, memory_keys=memory_keys, memory_values=memory_values, attention_mask=attention_mask, Wq=Wq, Wout=Wout, ln_gamma=ln_gamma, ln_beta=ln_beta)
    _L0_xattn_all = _L0_xattn_setup()
    _L0_xattn_in = {k: v for k, v in _L0_xattn_all.items() if k in ('Wq', 'Wout', 'ln_gamma', 'ln_beta')}
    del _L0_xattn_all
    return {'x': x, 'ctx_4096': ctx_4096, 'mask_BxS2_bf1': mask_BxS2_bf1, 'L0_xattn_Wq': _L0_xattn_in['Wq'], 'L0_xattn_Wout': _L0_xattn_in['Wout'], 'L0_xattn_ln_gamma': _L0_xattn_in['ln_gamma'], 'L0_xattn_ln_beta': _L0_xattn_in['ln_beta']}

def reference(x, ctx_4096, mask_BxS2_bf1, L0_xattn_Wq, L0_xattn_Wout, L0_xattn_ln_gamma, L0_xattn_ln_beta):
    import jax
    import jax.numpy as jnp

    def _L0_xattn_ref(hidden_states, memory_keys, memory_values, attention_mask, Wq, Wout, ln_gamma, ln_beta):
        import jax, jax.numpy as jnp
        import numpy as np
        HIDDEN = 512
        HEADS = 32
        HEAD_DIM = HIDDEN // HEADS
        LN_EPS = 1e-05

        def _split_heads(x):
            B, S, _ = x.shape
            return x.reshape(B, S, HEADS, HEAD_DIM).transpose(0, 2, 1, 3)
        residual = hidden_states
        mu = jnp.mean(hidden_states, axis=-1, keepdims=True)
        var = jnp.var(hidden_states, axis=-1, keepdims=True)
        x = (hidden_states - mu) * jax.lax.rsqrt(var + LN_EPS) * ln_gamma + ln_beta
        Q = _split_heads(x @ Wq.T)
        K = _split_heads(memory_keys)
        V = _split_heads(memory_values)
        scale = HEAD_DIM ** (-0.5)
        scores = jnp.einsum('bhsd,bhtd->bhst', Q, K) * scale
        mask = attention_mask[:, None, None, :]
        scores = jnp.where(mask, scores, -jnp.inf)
        probs = jax.nn.softmax(scores, axis=-1)
        attn = jnp.einsum('bhst,bhtd->bhsd', probs, V)
        B, _, S, _ = attn.shape
        attn = attn.transpose(0, 2, 1, 3).reshape(B, S, HIDDEN)
        out = attn @ Wout.T
        return residual + out
    x = _L0_xattn_ref(x, ctx_4096, ctx_4096, mask_BxS2_bf1, L0_xattn_Wq, L0_xattn_Wout, L0_xattn_ln_gamma, L0_xattn_ln_beta)
    return x

_drawn_inputs = setup_inputs


def setup_inputs(seed=0):
    import zlib

    import numpy as np

    out = dict(_drawn_inputs(seed))
    spreads = {'L0_xattn_ln_gamma': (1.0, 0.2), 'L0_xattn_ln_beta': (0.0, 0.315)}
    factors = {}
    for name, (base, spread) in spreads.items():
        noise = np.random.default_rng([zlib.crc32(name.encode()), seed]).standard_normal(out[name].shape)
        drawn = base * np.exp(spread * noise) if base else spread * noise
        out[name] = jnp.asarray(drawn.astype(out[name].dtype))
    for name, factor in factors.items():
        out[name] = (out[name] * factor).astype(out[name].dtype)
    return out
```

```python
import concourse.bass as bass
from concourse import mybir
from contextlib import ExitStack

F32 = mybir.dt.float32
BF16 = mybir.dt.bfloat16
ALU = mybir.AluOpType
ACT = mybir.ActivationFunctionType
AX_X = mybir.AxisListType.X

BATCH, QUERIES, HIDDEN = 32, 56, 512
CONTEXT, HEADS = 1500, 32
HEAD_DIM = HIDDEN // HEADS
SCALE = float(HEAD_DIM) ** -0.5
LN_EPS = 1e-5
PAIR = 2 * HEAD_DIM
PAIRS = HEADS // 2
PAIR_Q = 2 * QUERIES
SLOTS, LANES = 12, 125
CHUNKS, CHUNK = 3, 4
BLOCKS = 4
TAIL = LANES - 32 * (BLOCKS - 1)
GROUPS = 6
QUAD_PAIRS = [6, 6, 4]
GROUP_PAIRS = [3, 3, 3, 3, 2, 2]
GROUP_AT = [sum(GROUP_PAIRS[:g]) * PAIR_Q for g in range(GROUPS)]
KEY_ROWS = 96
MAX_ROW, MASK_ROW, ROWS = 96, 97, 98
ALL_Q = HEADS * QUERIES
UNITS = 3
QUADS = 8
QUAD_Q = 4 * QUERIES
MASKED = 1e38
X_TILES = BATCH * QUERIES // PAIR_Q
KC = HIDDEN // 128
TQ, TQ_TILES = 4, 4
TQ_COLS = TQ_TILES * PAIR_Q
TILES = CHUNKS * PAIRS
FIRST_TILE_SLOT, TILES_PER_SLOT = 3, 6
TURNS = {0: [(0, 0), (0, 1), (0, 2), (0, 3)], 2: [(1, 0), (1, 1), (1, 2)], 3: [(1, 3)],
         4: [(2, 0), (2, 1)], 5: [(2, 2), (2, 3)]}
CASTS = {1: 0, 4: 1, 6: 2}
MAX_SLOT = 11


def pair_at(j):
    q, g = j // 6, j % 6
    return GROUP_AT[g] + q * PAIR_Q


def positions():
    return sorted(range(PAIRS), key=pair_at)


def build(nc, x, ctx, mask, wq, wout, gamma, beta, out):
    with ExitStack() as stack:
        def sb(name, shape, dt=F32):
            return stack.enter_context(nc.sbuf_tensor(name, shape, dt))

        def sem(name):
            return stack.enter_context(nc.semaphore(name))

        q_all = nc.dram_tensor("q_all", [HIDDEN, BATCH * QUERIES], F32, kind="Internal").ap()
        key_rows = nc.dram_tensor("key_rows", [BATCH, 2, SLOTS * 128], F32, kind="Internal").ap()

        kT = sb("kT", [128, 2, CHUNKS, GROUPS, CHUNK, 128])
        kTb = sb("kTb", [128, 2, GROUPS, CHUNK, 128], BF16)
        k_src = sb("k_src", [128, 2, BLOCKS, CHUNK, GROUPS * PAIR])
        v = sb("v", [128, CHUNKS, CHUNK, HIDDEN])
        probs = sb("probs", [128, 3, ALL_Q])
        prob_sum = sb("prob_sum", [128, ALL_Q])
        qd = sb("qd", [128, 2, ALL_Q])
        qdb = sb("qdb", [128, ALL_Q], BF16)
        woutT = sb("woutT", [128, KC, HIDDEN])
        ident = sb("ident", [128, 128])
        ones = sb("ones", [128, 64])
        block_of = sb("block_of", [128, 8])
        own_head = sb("own_head", [128, 4])
        tile_max = sb("tile_max", [128, CHUNKS, PAIRS])
        neg_max = sb("neg_max", [128, PAIRS])
        neg_maxT = sb("neg_maxT", [16, PAIR_Q])
        head_sel = sb("head_sel", [128, KC, QUERIES])
        den_sel = sb("den_sel", [128, KC, QUERIES])
        den_inv = sb("den_inv", [128, KC, QUERIES])
        attnT = sb("attnT", [128, KC, PAIR_Q])
        x_res = sb("x_res", [128, HIDDEN])
        result = sb("result", [128, HIDDEN])
        stats = sb("stats", [128, X_TILES, 6])
        mean_var = sb("mean_var", [128, X_TILES, 2])
        rstd = sb("rstd", [128, X_TILES])
        gb = sb("gb", [128, 2, KC])
        mask_u8 = sb("mask_u8", [BATCH, CONTEXT], mybir.dt.uint8)

        kT_flat = kT[:].rearrange("p a c g k m -> p (a c g k m)")
        x_all = kT_flat[:, 0:X_TILES * HIDDEN].rearrange("p (i n) -> p i n", i=X_TILES)
        xT_at = X_TILES * HIDDEN
        xT = kT_flat[:, xT_at:xT_at + KC * X_TILES * PAIR_Q].rearrange("p (c n) -> p c n", c=KC)
        wqT_at = xT_at + KC * X_TILES * PAIR_Q
        wqT = kT_flat[:, wqT_at:wqT_at + KC * HIDDEN].rearrange("p (c n) -> p c n", c=KC)
        p_flat = probs[:].rearrange("p r n -> p (r n)")
        w_nat = p_flat[:, 0:2 * KC * HIDDEN].rearrange("p (w c n) -> p w c n", w=2, c=KC)
        qT_out = v[:, 2].rearrange("p k n -> p (k n)")[:, 0:KC * TQ_COLS].rearrange("p (c n) -> p c n", c=KC)
        mask_rows = prob_sum[0:BATCH, 0:SLOTS * 128].rearrange("p (k m) -> p k m", k=SLOTS)
        one_rows = qd[0:BATCH, 0, 0:SLOTS * 128]

        ps = stack.enter_context(nc.psum_tensor("ps", [128, 8, 512], F32))
        score_banks = [ps[:, 0:2, :], ps[:, 2:4, :]]
        head_acc = ps[:, 4:6, :].rearrange("p b n -> p (b n)").rearrange("p (r n) -> p r n", r=KC)
        den_acc = ps[:, 6:8, :].rearrange("p b n -> p (b n)").rearrange("p (r n) -> p r n", r=KC)
        aux = [ps[:, 6, :], ps[:, 7, :]]

        x_landed = [sem(f"x_landed{i}") for i in range(TQ)]
        w_landed = [sem("wq_landed"), sem("wout_landed")]
        gb_landed = sem("gb_landed")
        mask_landed = sem("mask_landed")
        rows_ready = sem("rows_ready")
        rows_stored = sem("rows_stored")
        zeroed = sem("zeroed")
        consts = sem("consts")
        ln_steps = sem("ln_steps")
        var_ready = sem("var_ready")
        std_ready = sem("std_ready")
        x_normed = sem("x_normed")
        pro_filled = sem("pro_filled")
        pro_drained = sem("pro_drained")
        q_stored = [sem(f"q_stored{i}") for i in range(TQ)]
        src_landed = [sem("src_landed0"), sem("src_landed1")]
        kT_turned = sem("kT_turned")
        rows_landed = [sem("rows_landed0"), sem("rows_landed1")]
        v_landed = [sem(f"v_landed{c}") for c in range(CHUNKS)]
        q_landed = [sem("q_landed0"), sem("q_landed1")]
        qdb_cast = sem("qdb_cast")
        kTb_cast = sem("kTb_cast")
        tile_scored = sem("tile_scored")
        tile_taken = sem("tile_taken")
        max_ready = sem("max_ready")
        max_turned = sem("max_turned")
        max_copied = sem("max_copied")
        max_landed = sem("max_landed")
        unit_scored = sem("unit_scored")
        unit_exped = sem("unit_exped")
        pv_done = sem("pv_done")
        summed = sem("summed")
        den_scored = sem("den_scored")
        den_taken = sem("den_taken")
        heads_taken = sem("heads_taken")
        own_steps = sem("own_steps")
        attn_ready = sem("attn_ready")
        projected = sem("projected")
        res_landed = sem("res_landed")
        result_ready = sem("result_ready")
        result_stored = sem("result_stored")

        OWN = 7

        def nth(per, bt, extra):
            return bt[0] * (2 * per) + (per * bt[1] + extra)

        def nonzero(count):
            return not isinstance(count, int) or count > 0

        def after(bt, n):
            return (bt[0], bt[1] + n)

        def row0(ap2, bt, size):
            return ap2[bass.ds(bt[0] * 2 + bt[1], size)]

        def load_k_src(sp, bt, c):
            n = 3 * bt[1] + c
            src = row0(ctx, bt, 1).rearrange("a (m k) n -> m (a k) n", k=SLOTS)
            for q in range(3):
                w = QUAD_PAIRS[q] * PAIR
                cols = slice(GROUPS * PAIR * q, GROUPS * PAIR * q + w)
                for b in range(BLOCKS - 1):
                    sp.dma_start(k_src[32 * q:32 * q + 32, n % 2, b, :, 0:w],
                                 src[32 * b:32 * b + 32, CHUNK * c:CHUNK * c + CHUNK, cols]
                                 ).then_inc(src_landed[n % 2], 16)
                b = BLOCKS - 1
                for lo, hi in ((0, 16), (16, TAIL)):
                    sp.dma_start(k_src[32 * q + lo:32 * q + hi, n % 2, b, :, 0:w],
                                 src[32 * b + lo:32 * b + hi, CHUNK * c:CHUNK * c + CHUNK, cols]
                                 ).then_inc(src_landed[n % 2], 16)
        SRC_DMAS = 3 * (BLOCKS - 1 + 2)

        def load_v(sp, bt, c):
            src = row0(ctx, bt, 1).rearrange("a (m k) n -> m (a k) n", k=SLOTS)
            for lo, hi in ((112, LANES), (0, 112)):
                sp.dma_start(v[lo:hi, c], src[lo:hi, CHUNK * c:CHUNK * c + CHUNK, :]).then_inc(v_landed[c], 16)

        def load_rows(sp, bt):
            src = row0(key_rows, bt, 1).rearrange("a r (c n) -> (a r) c n", c=CHUNKS)
            for c in range(CHUNKS):
                for g in range(GROUPS):
                    dst = kT[MAX_ROW:ROWS, bt[1] % 2, c, g].rearrange("p k m -> p (k m)")
                    sp.dma_start(dst, src[:, c, :]).then_inc(rows_landed[bt[1] % 2], 16)
        ROW_DMAS = CHUNKS * GROUPS

        def load_q(sp, bt):
            p = bt[1] % 2
            src = q_all.rearrange("(j e d) s -> e d j s", e=2, d=HEAD_DIM)
            here = bass.ds(bt[0] * (2 * QUERIES) + bt[1] * QUERIES, QUERIES)
            for q in range(3):
                for e in range(2):
                    r0, at = 32 * q + HEAD_DIM * e, q * PAIR_Q + e * QUERIES
                    for g0, g1 in ((0, 4), (4, 6)):
                        if g0 >= QUAD_PAIRS[q]:
                            continue
                        w = GROUP_PAIRS[g0] * PAIR_Q
                        dst = qd[r0:r0 + HEAD_DIM, p, GROUP_AT[g0]:GROUP_AT[g0] + (g1 - g0) * w]
                        dst = dst.rearrange("p (g n) -> p g n", g=g1 - g0)[:, :, at:at + QUERIES]
                        sp.dma_start(dst, src[e][:, 6 * q + g0:6 * q + g1, here]).then_inc(q_landed[p], 16)
        Q_DMAS = 2 * (2 + 2 + 1)

        def load_max(sp, bt):
            sp.wait_ge(max_copied, nth(1, bt, 1))
            sp.dma_start(qd[MAX_ROW:MAX_ROW + 1, bt[1] % 2].rearrange("p (j n) -> p j n", j=PAIRS),
                         neg_maxT[:, :]).then_inc(max_landed, 16)

        def turn(dve, bt, c, k):
            n = 3 * bt[1] + c
            if k == 0:
                dve.wait_ge(src_landed[n % 2], bt[0] * (3 * 16 * SRC_DMAS) + 16 * SRC_DMAS * (n // 2 + 1))
                free = nth(UNITS * SLOTS, bt, UNITS * (CHUNK * (c + 1) - 2 * SLOTS))
                if nonzero(free):
                    dve.wait_ge(unit_scored, free)
            src = k_src[0:KEY_ROWS, n % 2, :, k, :].rearrange("p b (g n) -> p g b n", g=GROUPS)
            dst = kT[0:KEY_ROWS, bt[1] % 2, c, :, k, :].rearrange("p g (b n) -> p g b n", b=BLOCKS)
            ins = nc.vector.transpose(dst, src)
            if k == CHUNK - 1:
                ins.then_inc(kT_turned, 1)

        def cast_q(act, bt):
            act.wait_ge(q_landed[bt[1] % 2], bt[0] * (16 * Q_DMAS) + 16 * Q_DMAS * (bt[1] // 2 + 1))
            used = nth(TILES, bt, 0)
            if nonzero(used):
                act.wait_ge(tile_scored, used)
            nc.scalar.copy(qdb[0:KEY_ROWS, :], qd[0:KEY_ROWS, bt[1] % 2, :]).then_inc(qdb_cast, 1)

        def cast_k(act, bt, c, half):
            n = 3 * bt[1] + c
            if half == 0:
                act.wait_ge(kT_turned, nth(CHUNKS, bt, c + 1))
                act.wait_ge(rows_landed[bt[1] % 2], bt[0] * (16 * ROW_DMAS) + 16 * ROW_DMAS * (bt[1] // 2 + 1))
                used = nth(TILES, bt, PAIRS * (c - 1))
                if nonzero(used):
                    act.wait_ge(tile_scored, used)
            gs = slice(3 * half, 3 * half + 3)
            ins = nc.scalar.copy(kTb[0:ROWS, n % 2, gs], kT[0:ROWS, bt[1] % 2, c, gs])
            if half == 1:
                ins.then_inc(kTb_cast, 1)

        def score_tile(pe, bt, i):
            c, at = i // PAIRS, i % PAIRS
            if i == 0:
                pe.wait_ge(qdb_cast, nth(1, bt, 1))
                for s, value in ((den_taken, nth(1, bt, -1)), (max_copied, nth(1, bt, 0))):
                    if nonzero(value):
                        pe.wait_ge(s, value)
                if bt[1] % 2 == 1:
                    if nonzero(bt[0]):
                        pe.wait_ge(result_ready, bt[0])
            if at == 0:
                pe.wait_ge(kTb_cast, nth(CHUNKS, bt, c + 1))
            free = nth(TILES, bt, i - 1)
            if nonzero(free):
                pe.wait_ge(tile_taken, free)
            g = positions()[at] % 6
            n = 3 * bt[1] + c
            nc.tensor.matmul(aux[i % 2][0:PAIR_Q, 0:CHUNK * LANES], qdb[0:ROWS, at * PAIR_Q:(at + 1) * PAIR_Q],
                             kTb[0:ROWS, n % 2, g, :, 0:LANES], start=True, stop=True).then_inc(tile_scored, 1)

        def take_tile(dve, bt, i):
            dve.wait_ge(tile_scored, nth(TILES, bt, i + 1))
            nc.vector.tensor_reduce(tile_max[0:PAIR_Q, i // PAIRS, i % PAIRS:i % PAIRS + 1],
                                    aux[i % 2][0:PAIR_Q, 0:CHUNK * LANES], AX_X, ALU.max).then_inc(tile_taken, 1)

        def take_max(dve, bt):
            dve.wait_ge(tile_taken, nth(TILES, bt, TILES))
            if nonzero(nth(1, bt, 0)):
                dve.wait_ge(max_turned, nth(1, bt, 0))
            nc.vector.tensor_reduce(neg_max[0:PAIR_Q, :], tile_max[0:PAIR_Q].rearrange("p c j -> p j c"),
                                    AX_X, ALU.max, negate=True).then_inc(max_ready, 1)

        def turn_max(pe, bt):
            pe.wait_ge(max_ready, nth(1, bt, 1))
            nc.tensor.transpose(aux[0][0:PAIRS, 0:PAIR_Q], neg_max[0:PAIR_Q, :],
                                ident[0:PAIR_Q, 0:PAIR_Q]).then_inc(max_turned, 1)

        def copy_max(act, bt):
            act.wait_ge(max_turned, nth(1, bt, 1))
            if nonzero(nth(16, bt, 0)):
                act.wait_ge(max_landed, nth(16, bt, 0))
            nc.scalar.copy(neg_maxT[:, :], aux[0][0:PAIRS, 0:PAIR_Q]).then_inc(max_copied, 1)

        def score_unit(pe, bt, k, u):
            p, c = bt[1] % 2, k // CHUNK
            if k == 0 and u == 0:
                pe.wait_ge(max_landed, nth(16, bt, 16))
            if k % CHUNK == 0 and u == 0:
                pe.wait_ge(kT_turned, nth(CHUNKS, bt, c + 1))
            unit = UNITS * k + u
            free = nth(UNITS * SLOTS, bt, unit - 1)
            if nonzero(free):
                pe.wait_ge(unit_exped, free)
            for i in range(2):
                g = 2 * u + i
                w = GROUP_PAIRS[g] * PAIR_Q
                mm = nc.tensor.matmul(score_banks[unit % 2][0:LANES, i, 0:w],
                                      kT[0:ROWS, p, c, g, k % CHUNK, 0:LANES],
                                      qd[0:ROWS, p, GROUP_AT[g]:GROUP_AT[g] + w], start=True, stop=True)
            mm.then_inc(unit_scored, 1)

        def exp_unit(act, bt, k, u):
            unit = UNITS * k + u
            if u == 0:
                if nonzero(nth(SLOTS, bt, k - 2)):
                    act.wait_ge(pv_done, nth(SLOTS, bt, k - 2))
                used = nth(SLOTS - 1, bt, max(k - 3, 1) if k >= 3 else k - 2)
                if nonzero(used):
                    act.wait_ge(summed, used)
            act.wait_ge(unit_scored, nth(UNITS * SLOTS, bt, unit + 1))
            w = GROUP_PAIRS[2 * u] * PAIR_Q
            at = GROUP_AT[2 * u]
            nc.scalar.activation(probs[0:LANES, k % 3, at:at + 2 * w].rearrange("p (b n) -> p b n", b=2),
                                 score_banks[unit % 2][0:LANES, :, 0:w], ACT.Exp, scale=SCALE
                                 ).then_inc(unit_exped, 1)

        def pv_part(pe, bt, k, half):
            c = k // CHUNK
            if half == 0:
                pe.wait_ge(unit_exped, nth(UNITS * SLOTS, bt, UNITS * (k + 1)))
                if k % CHUNK == 0:
                    pe.wait_ge(v_landed[c], nth(32, bt, 32))
                if k == 0 and nonzero(nth(1, bt, 0)):
                    pe.wait_ge(heads_taken, nth(1, bt, 0))
            for u in range(4 * half, 4 * half + 4):
                lo = 64 * (u % 2)
                mm = nc.tensor.matmul(head_acc[lo:lo + 64, u // 2, 0:QUAD_Q],
                                      v[0:LANES, c, k % CHUNK, 64 * u:64 * u + 64],
                                      quad(probs, k % 3, u), start=(k == 0 and (u // 2) % 2 == 0),
                                      stop=(k == SLOTS - 1), skip_group_check=True)
            if half == 1:
                mm.then_inc(pv_done, 1)

        def quad(tile, r, u):
            a, b = pair_at(2 * u), pair_at(2 * u + 1)
            step = b - a
            flat = tile[0:LANES].rearrange("p r n -> p (r n)") if r is not None else tile[0:LANES, :]
            at = a + (ALL_Q * r if r is not None else 0)
            two = flat[:, at:at + step + PAIR_Q]
            return bass.AP(two.tensor, two.offset, [list(two.ap[0]), [step, 2], [1, PAIR_Q]])

        def add_probs(pool, bt, k):
            pool.wait_ge(unit_exped, nth(UNITS * SLOTS, bt, UNITS * (k + 1)))
            if k == 1:
                if nonzero(nth(1, bt, 0)):
                    pool.wait_ge(den_scored, nth(1, bt, 0))
            else:
                pool.wait_ge(summed, nth(SLOTS - 1, bt, k - 1))
            first = probs[0:LANES, 0, :] if k == 1 else prob_sum[0:LANES, :]
            nc.gpsimd.tensor_tensor(prob_sum[0:LANES, :], first, probs[0:LANES, k % 3, :],
                                    ALU.add).then_inc(summed, 1)

        def score_den(pe, bt):
            pe.wait_ge(summed, nth(SLOTS - 1, bt, SLOTS - 1))
            if not (isinstance(bt[0], int) and nth(1, bt, 1) == BATCH):
                pe.wait_ge(max_copied, nth(1, bt, 2))
            if nonzero(nth(1, bt, 0)):
                pe.wait_ge(den_taken, nth(1, bt, 0))
            double = bt[0] + bt[1] // 2
            if bt[1] % 2 == 1 and nonzero(double):
                pe.wait_ge(result_ready, double)
            for u in range(QUADS):
                lo = 64 * (u % 2)
                mm = nc.tensor.matmul(den_acc[lo:lo + 64, u // 2, 0:QUAD_Q], ones[0:LANES, :],
                                      quad(prob_sum, None, u), start=True, stop=True)
            mm.then_inc(den_scored, 1)

        def own_heads(dve, acc, dst, first_step, done):
            for e in range(4):
                src = acc[:, :, QUERIES * e:QUERIES * (e + 1)]
                if e == 0:
                    nc.vector.tensor_scalar(dst[:], src, own_head[:, 0:1], None, ALU.mult).then_inc(own_steps, 1)
                    continue
                dve.wait_ge(own_steps, first_step + e - 1)
                ins = nc.vector.scalar_tensor_tensor(dst[:], src, own_head[:, e:e + 1], dst[:], ALU.mult, ALU.add)
                ins.then_inc(own_steps if e < 3 else done, 1)

        def finish_heads(dve, bt):
            if nonzero(nth(1, bt, 0)):
                dve.wait_ge(attn_ready, nth(1, bt, 0))
            dve.wait_ge(pv_done, nth(SLOTS, bt, SLOTS))
            own_heads(dve, head_acc, head_sel, nth(OWN, bt, 1), heads_taken)
            dve.wait_ge(den_scored, nth(1, bt, 1))
            own_heads(dve, den_acc, den_sel, nth(OWN, bt, 4), den_taken)
            dve.wait_ge(den_taken, nth(1, bt, 1))
            nc.vector.reciprocal(den_inv[:], den_sel[:]).then_inc(own_steps, 1)
            dve.wait_ge(own_steps, nth(OWN, bt, OWN))
            dve.wait_ge(heads_taken, nth(1, bt, 1))
            if bt[1] % 2 == 0 and nonzero(bt[0] + bt[1] // 2):
                dve.wait_ge(projected, bt[0] + bt[1] // 2)
            at = QUERIES * (bt[1] % 2)
            nc.vector.tensor_tensor(attnT[:, :, at:at + QUERIES], head_sel[:], den_inv[:],
                                    ALU.mult).then_inc(attn_ready, 1)

        def project_out(pe, bt):
            pe.wait_ge(attn_ready, nth(1, bt, 1))
            pe.wait_ge(den_taken, nth(1, bt, 1))
            for c in range(KC):
                mm = nc.tensor.matmul(aux[0][0:PAIR_Q, :], attnT[:, c, :], woutT[:, c, :],
                                      start=(c == 0), stop=(c == KC - 1))
            mm.then_inc(projected, 1)

        def add_residual(dve, i):
            dve.wait_ge(projected, i + 1)
            dve.wait_ge(res_landed, i * 16 + 16)
            if nonzero(i):
                dve.wait_ge(result_stored, i * 16)
            nc.vector.tensor_tensor(result[0:PAIR_Q, :], aux[0][0:PAIR_Q, :], x_res[0:PAIR_Q, :],
                                    ALU.add).then_inc(result_ready, 1)

        x_rows = x.rearrange("(i b) s n -> i (b s) n", b=2)
        out_rows = out.rearrange("(i b) s n -> i (b s) n", b=2)

        def load_residual(sp, i):
            if nonzero(i):
                sp.wait_ge(result_ready, i)
            sp.dma_start(x_res[0:PAIR_Q, :], x_rows[bass.ds(i, 1)].rearrange("a p n -> (a p) n")
                         ).then_inc(res_landed, 16)

        def store_result(sp, i):
            sp.wait_ge(result_ready, i + 1)
            sp.dma_start(out_rows[bass.ds(i, 1)].rearrange("a p n -> (a p) n"), result[0:PAIR_Q, :]
                         ).then_inc(result_stored, 16)

        def loop(eng, body):
            body(0, first=True, last=False)
            with eng.Fori(1, BATCH // 2 - 1) as i:
                body(i, first=False, last=False)
            body(BATCH // 2 - 1, first=False, last=True)

        block = stack.enter_context(nc.Block())

        @block.sync
        def _(sp):
            x_tiles = x_rows.rearrange("i p n -> p i n")
            sp.dma_start(gb[:, 0, :], gamma.rearrange("(c p) -> p c", p=128),
                         allow_slow_non_contiguous=True).then_inc(gb_landed, 16)
            sp.dma_start(gb[:, 1, :], beta.rearrange("(c p) -> p c", p=128),
                         allow_slow_non_contiguous=True).then_inc(gb_landed, 16)
            sp.dma_start(w_nat[:, 0], wq.rearrange("(c p) n -> p c n", p=128)).then_inc(w_landed[0], 16)
            for i in range(TQ):
                t = slice(TQ_TILES * i, TQ_TILES * (i + 1))
                sp.dma_start(x_all[0:PAIR_Q, t], x_tiles[:, t]).then_inc(x_landed[i], 16)
            sp.dma_start(mask_u8[:, :], mask).then_inc(mask_landed, 16)
            sp.dma_start(w_nat[:, 1], wout.rearrange("(c p) n -> p c n", p=128)).then_inc(w_landed[1], 16)
            b0 = (0, 0)
            sp.wait_ge(zeroed, 1)
            load_k_src(sp, b0, 0)
            load_k_src(sp, b0, 1)
            load_v(sp, b0, 0)
            load_v(sp, b0, 1)
            sp.wait_ge(rows_ready, 1)
            sp.dma_start(key_rows[:, 1, :], mask_rows.rearrange("p k m -> p (k m)")).then_inc(rows_stored, 16)
            sp.dma_start(key_rows[:, 0, :], one_rows).then_inc(rows_stored, 16)
            for i in range(TQ):
                for c in range(KC):
                    sp.wait_ge(pro_drained, Q_UNIT(i, c) + 1)
                    sp.dma_start(q_all[128 * c:128 * (c + 1), TQ_COLS * i:TQ_COLS * (i + 1)],
                                 qT_out[:, c, :]).then_inc(q_stored[i], 16)
            for i in range(TQ):
                sp.wait_ge(q_stored[i], 16 * KC)
            sp.wait_ge(rows_stored, 32)
            sp.wait_ge(pro_filled, PRO_UNITS)
            load_rows(sp, b0)
            sp.wait_ge(zeroed, 2)
            load_q(sp, b0)
            load_v(sp, b0, 2)
            sp.wait_ge(kT_turned, 1)
            load_k_src(sp, b0, 2)
            sp.wait_ge(kT_turned, 2)
            load_k_src(sp, (0, 1), 0)
            sp.wait_ge(kT_turned, 3)
            load_k_src(sp, (0, 1), 1)
            load_max(sp, b0)

            def body(i, first, last):
                for o in range(2):
                    bt, nxt = (i, o), (i, o + 1)
                    final = last and o == 1
                    if not (first and o == 0):
                        sp.wait_ge(pv_done, nth(SLOTS, bt, 0))
                        load_v(sp, bt, 2)
                        sp.wait_ge(unit_scored, nth(UNITS * SLOTS, bt, 0))
                    if o == 1:
                        load_residual(sp, i)
                    if not final:
                        load_rows(sp, nxt)
                        load_q(sp, nxt)
                        sp.wait_ge(kT_turned, nth(CHUNKS, nxt, 1))
                        load_k_src(sp, nxt, 2)
                    if o == 0 and not first:
                        store_result(sp, i - 1)
                    if not last:
                        sp.wait_ge(kT_turned, nth(CHUNKS, nxt, 2))
                        load_k_src(sp, after(nxt, 1), 0)
                    if not final:
                        sp.wait_ge(pv_done, nth(SLOTS, bt, CHUNK))
                        load_v(sp, nxt, 0)
                    if not last:
                        sp.wait_ge(kT_turned, nth(CHUNKS, nxt, 3))
                        load_k_src(sp, after(nxt, 1), 1)
                    if not final:
                        sp.wait_ge(pv_done, nth(SLOTS, bt, 2 * CHUNK))
                        load_v(sp, nxt, 1)
                        load_max(sp, nxt)

            loop(sp, body)
            store_result(sp, BATCH // 2 - 1)
            sp.wait_ge(result_stored, 16 * (BATCH // 2))

        @block.gpsimd
        def _(pool):
            nc.gpsimd.memset(ident[:], 0.0).then_inc(consts, 1)
            pool.wait_ge(consts, 1)
            nc.gpsimd.memset(block_of[:], 1.0).then_inc(consts, 1)
            pool.wait_ge(consts, 2)
            nc.gpsimd.affine_select(out=ident[:], in_=ident[:], compare_op=ALU.not_equal, fill=1.0, base=0,
                                    pattern=[[-1, 128]], channel_multiplier=1).then_inc(consts, 1)
            pool.wait_ge(consts, 3)
            nc.gpsimd.affine_select(out=block_of[:], in_=block_of[:], compare_op=ALU.is_ge, fill=0.0, base=0,
                                    pattern=[[-HEAD_DIM, 8]], channel_multiplier=1).then_inc(consts, 1)
            pool.wait_ge(consts, 4)
            nc.gpsimd.affine_select(out=block_of[:], in_=block_of[:], compare_op=ALU.is_ge, fill=0.0,
                                    base=HEAD_DIM - 1, pattern=[[HEAD_DIM, 8]],
                                    channel_multiplier=-1).then_inc(consts, 1)
            pool.wait_ge(consts, 5)
            nc.gpsimd.tensor_tensor(own_head[:], block_of[:, 0:4], block_of[:, 4:8], ALU.add).then_inc(consts, 1)
            pool.wait_ge(consts, 6)
            nc.gpsimd.memset(ones[:], 1.0).then_inc(consts, 1)
            pool.wait_ge(consts, 7)
            pool.wait_ge(rows_stored, 32)
            nc.gpsimd.memset(qd[MAX_ROW:ROWS], 2.0).then_inc(consts, 1)
            pool.wait_ge(consts, 8)
            nc.gpsimd.memset(qdb[MAX_ROW:ROWS, :], 1.0).then_inc(consts, 1)
            pool.wait_ge(consts, 9)
            nc.gpsimd.memset(qdb[MAX_ROW:MAX_ROW + 1, :], 0.0).then_inc(consts, 1)

            pool.wait_ge(consts, 10)

            def body(i, first, last):
                for o in range(2):
                    for k in range(1, SLOTS):
                        add_probs(pool, (i, o), k)

            loop(pool, body)

        @block.vector
        def _(dve):
            nc.vector.memset(k_src[0:KEY_ROWS], 0.0).then_inc(zeroed, 1)
            nc.vector.memset(mask_rows, 0.0).then_inc(ln_steps, 1)
            nc.vector.memset(one_rows, 1.0)
            dve.wait_ge(mask_landed, 16)
            dve.wait_ge(ln_steps, 1)
            nc.vector.tensor_scalar(mask_rows[:, :, 0:LANES], mask_u8[:, :].rearrange("p (m k) -> p k m", k=SLOTS),
                                    MASKED, -MASKED, ALU.mult, ALU.add).then_inc(rows_ready, 1)
            for i in range(TQ):
                dve.wait_ge(x_landed[i], 16)
                tiles = range(TQ_TILES * i, TQ_TILES * (i + 1))
                t4 = slice(TQ_TILES * i, TQ_TILES * (i + 1))
                for t in tiles:
                    ins = nc.vector.bn_stats(stats[0:PAIR_Q, t, :], x_all[0:PAIR_Q, t, :])
                ins.then_inc(ln_steps, 1)
                dve.wait_ge(ln_steps, 4 * i + 2)
                for t in tiles:
                    ins = nc.vector.bn_aggr(mean_var[0:PAIR_Q, t, :], stats[0:PAIR_Q, t, :])
                ins.then_inc(ln_steps, 1)
                dve.wait_ge(ln_steps, 4 * i + 3)
                nc.vector.tensor_scalar(rstd[0:PAIR_Q, t4], mean_var[0:PAIR_Q, t4, 1], LN_EPS, None,
                                        ALU.add).then_inc(var_ready, 1)
                dve.wait_ge(std_ready, i + 1)
                nc.vector.reciprocal(rstd[0:PAIR_Q, t4], rstd[0:PAIR_Q, t4]).then_inc(ln_steps, 1)
                dve.wait_ge(ln_steps, 4 * i + 4)
                for t in tiles:
                    ins = nc.vector.tensor_scalar(x_all[0:PAIR_Q, t, :], x_all[0:PAIR_Q, t, :],
                                                  mean_var[0:PAIR_Q, t, 0:1], rstd[0:PAIR_Q, t:t + 1],
                                                  ALU.subtract, ALU.mult)
                ins.then_inc(x_normed, 1)
                nc.vector.memset(stats[0:PAIR_Q, 0, 0:1], 0.0).then_inc(ln_steps, 1)
            dve.wait_ge(rows_stored, 32)
            nc.vector.memset(qd[0:KEY_ROWS], 0.0).then_inc(zeroed, 1)
            dve.wait_ge(pro_filled, PRO_UNITS)
            b0 = (0, 0)
            for c in range(CHUNKS):
                for k in range(CHUNK):
                    turn(dve, b0, c, k)
                for t in range(PAIRS):
                    take_tile(dve, b0, PAIRS * c + t)
            take_max(dve, b0)

            def body(i, first, last):
                for o in range(2):
                    bt, nxt = (i, o), (i, o + 1)
                    final = last and o == 1
                    for k in range(SLOTS):
                        if k == 1 and not (first and o == 0):
                            finish_heads(dve, after(bt, -1))
                        if k == 2 and o == 0 and not first:
                            add_residual(dve, i - 1)
                        if final:
                            continue
                        for c, kk in TURNS.get(k, []):
                            turn(dve, nxt, c, kk)
                        at = (k - FIRST_TILE_SLOT) * TILES_PER_SLOT
                        if 0 <= at < TILES:
                            for t in range(at, at + TILES_PER_SLOT):
                                take_tile(dve, nxt, t)
                        if k == MAX_SLOT - 1:
                            take_max(dve, nxt)

            loop(dve, body)
            finish_heads(dve, (BATCH // 2 - 1, 1))
            add_residual(dve, BATCH // 2 - 1)

        @block.scalar
        def _(act):
            def drain(unit, dst, scale=None, bias=None):
                act.wait_ge(pro_filled, unit + 1)
                src = ps[:, unit % 8, 0:dst.shape[-1]]
                if scale is None:
                    nc.scalar.copy(dst, src).then_inc(pro_drained, 1)
                else:
                    nc.scalar.activation(dst, src, ACT.Identity, bias=bias, scale=scale).then_inc(pro_drained, 1)

            for kind, a, b in PRO_PLAN:
                unit = _FILLS.index((kind, a, b)) if kind != "std" else None
                if kind == "wq":
                    drain(unit, wqT[:, a, :])
                elif kind == "wout":
                    drain(unit, woutT[:, a, :])
                elif kind == "xT":
                    if b == 0:
                        act.wait_ge(gb_landed, 32)
                    drain(unit, xT[:, b, TQ_COLS * a:TQ_COLS * (a + 1)], gb[:, 0, b:b + 1], gb[:, 1, b:b + 1])
                elif kind == "q":
                    if a >= 1:
                        act.wait_ge(q_stored[a - 1], 16 * KC)
                    drain(unit, qT_out[:, b, :])
                else:
                    act.wait_ge(var_ready, a + 1)
                    t4 = slice(TQ_TILES * a, TQ_TILES * (a + 1))
                    nc.scalar.activation(rstd[0:PAIR_Q, t4], rstd[0:PAIR_Q, t4], ACT.Sqrt).then_inc(std_ready, 1)
            b0 = (0, 0)
            act.wait_ge(consts, 10)
            cast_q(act, b0)
            for c in range(CHUNKS):
                cast_k(act, b0, c, 0)
                cast_k(act, b0, c, 1)
            copy_max(act, b0)

            def body(i, first, last):
                for o in range(2):
                    bt, nxt = (i, o), (i, o + 1)
                    final = last and o == 1
                    for k in range(SLOTS):
                        exp_unit(act, bt, k, 0)
                        if k == 1 and not final:
                            cast_q(act, nxt)
                        exp_unit(act, bt, k, 1)
                        if k == MAX_SLOT and not final:
                            copy_max(act, nxt)
                        if k in CASTS and not final:
                            cast_k(act, nxt, CASTS[k], 0)
                        exp_unit(act, bt, k, 2)
                        if k in CASTS and not final:
                            cast_k(act, nxt, CASTS[k], 1)

            loop(act, body)

        @block.tensor
        def _(pe):
            pe.wait_ge(consts, 10)
            n = 0
            for kind, a, b in PRO_PLAN:
                if kind == "std":
                    continue
                if n >= 8:
                    pe.wait_ge(pro_drained, n - 7)
                bank = ps[:, n % 8, :]
                if kind in ("wq", "wout"):
                    which = 0 if kind == "wq" else 1
                    pe.wait_ge(w_landed[which], 16)
                    for c in range(KC):
                        mm = nc.tensor.transpose(bank[:, 128 * c:128 * (c + 1)],
                                                 w_nat[:, which, c, 128 * a:128 * (a + 1)], ident[:, :])
                elif kind == "xT":
                    if b == 0:
                        pe.wait_ge(x_normed, a + 1)
                    for t in range(TQ_TILES):
                        mm = nc.tensor.transpose(bank[:, PAIR_Q * t:PAIR_Q * (t + 1)],
                                                 x_all[0:PAIR_Q, TQ_TILES * a + t, 128 * b:128 * (b + 1)],
                                                 ident[0:PAIR_Q, 0:PAIR_Q])
                else:
                    if b == 0:
                        pe.wait_ge(pro_drained, XT_UNIT(a, KC - 1) + 1)
                    for c in range(KC):
                        mm = nc.tensor.matmul(bank[:, 0:TQ_COLS], wqT[:, c, 128 * b:128 * (b + 1)],
                                              xT[:, c, TQ_COLS * a:TQ_COLS * (a + 1)],
                                              start=(c == 0), stop=(c == KC - 1))
                mm.then_inc(pro_filled, 1)
                n += 1
            pe.wait_ge(pro_drained, PRO_UNITS)
            b0 = (0, 0)
            for t in range(TILES):
                score_tile(pe, b0, t)
            turn_max(pe, b0)

            def body(i, first, last):
                for o in range(2):
                    bt, nxt, prev = (i, o), (i, o + 1), (i, o - 1)
                    final = last and o == 1
                    for k in range(SLOTS):
                        at = (k - FIRST_TILE_SLOT) * TILES_PER_SLOT
                        tiles = list(range(at, at + TILES_PER_SLOT)) if 0 <= at < TILES and not final else []
                        pv = (bt, k - 1) if k > 0 else (prev, SLOTS - 1)
                        has_pv = k > 0 or not (first and o == 0)
                        score_unit(pe, bt, k, 0)
                        for t in tiles[0:2]:
                            score_tile(pe, nxt, t)
                        if has_pv:
                            pv_part(pe, pv[0], pv[1], 0)
                        score_unit(pe, bt, k, 1)
                        for t in tiles[2:4]:
                            score_tile(pe, nxt, t)
                        if k == MAX_SLOT and not final:
                            turn_max(pe, nxt)
                        if has_pv:
                            pv_part(pe, pv[0], pv[1], 1)
                        score_unit(pe, bt, k, 2)
                        for t in tiles[4:6]:
                            score_tile(pe, nxt, t)
                        if k == 0 and not (first and o == 0):
                            score_den(pe, prev)
                        if k == 2 and o == 0 and not first:
                            project_out(pe, prev)

            loop(pe, body)
            end = (BATCH // 2 - 1, 1)
            pv_part(pe, end, SLOTS - 1, 0)
            pv_part(pe, end, SLOTS - 1, 1)
            score_den(pe, end)
            project_out(pe, end)


def _plan():
    plan = [("wq", c, 0) for c in range(KC)] + [("std", 0, 0)] + [("xT", 0, c) for c in range(KC)]
    for i in range(TQ):
        if i + 1 < TQ:
            plan += [("std", i + 1, 0)] + [("xT", i + 1, c) for c in range(KC)]
        plan += [("q", i, c) for c in range(KC)]
    return plan + [("wout", c, 0) for c in range(KC)]


PRO_PLAN = _plan()
_FILLS = [p for p in PRO_PLAN if p[0] != "std"]
PRO_UNITS = len(_FILLS)


def XT_UNIT(i, c):
    return _FILLS.index(("xT", i, c))


def Q_UNIT(i, c):
    return _FILLS.index(("q", i, c))


_INS = ["x", "ctx_4096", "mask_BxS2_bf1", "L0_xattn_Wq", "L0_xattn_Wout", "L0_xattn_ln_gamma", "L0_xattn_ln_beta"]


def kernel(**inputs):
    import numpy as np
    import concourse.bacc as bacc
    from concourse.bass_utils import run_bass_kernel_spmd

    nc = bacc.Bacc("TRN2", target_bir_lowering=False, num_devices=1)
    arrays, args = {}, []
    for name in _INS:
        a = np.ascontiguousarray(inputs[name])
        if a.dtype == np.bool_:
            a = a.view(np.uint8)
        arrays[f"in_{name}"] = a
        args.append(nc.dram_tensor(f"in_{name}", a.shape, mybir.dt.from_np(a.dtype), kind="ExternalInput").ap())
    out = nc.dram_tensor("out", [BATCH, QUERIES, HIDDEN], F32, kind="ExternalOutput").ap()
    build(nc, *args, out)
    r = run_bass_kernel_spmd(nc, [arrays], core_ids=[0])
    return r.results[0]["out"]
```

```python
import concourse.bass as bass
from concourse import mybir
from contextlib import ExitStack

F32 = mybir.dt.float32
BF16 = mybir.dt.bfloat16
ALU = mybir.AluOpType
ACT = mybir.ActivationFunctionType
AX_X = mybir.AxisListType.X

BATCH, QUERIES, HIDDEN = 32, 56, 512
CONTEXT, HEADS = 1500, 32
HEAD_DIM = HIDDEN // HEADS
SCALE = float(HEAD_DIM) ** -0.5
LN_EPS = 1e-5
PAIR = 2 * HEAD_DIM
PAIRS = HEADS // 2
PAIR_Q = 2 * QUERIES
SLOTS, LANES = 12, 125
CHUNKS, CHUNK = 3, 4
BLOCKS = 4
TAIL = LANES // BLOCKS
GROUPS = 6
QUAD_PAIRS = [6, 6, 4]
GROUP_PAIRS = [3, 3, 3, 3, 2, 2]
GROUP_AT = [sum(GROUP_PAIRS[:g]) * PAIR_Q for g in range(GROUPS)]
KEY_ROWS = 96
MAX_ROW, MASK_ROW, ROWS = 96, 97, 98
ALL_Q = HEADS * QUERIES
UNITS = 3
QUADS = 8
QUAD_Q = 4 * QUERIES
MASKED = 1e38
KC = HIDDEN // 128
TQ, TQ_TILES = 4, 4
TQ_COLS = TQ_TILES * PAIR_Q
TILES = CHUNKS * PAIRS
FIRST_TILE_SLOT, TILES_PER_SLOT = 3, 6
TURNS = {0: [(0, 0), (0, 1), (0, 2), (0, 3)], 2: [(1, 0), (1, 1), (1, 2), (1, 3)],
         4: [(2, 0), (2, 1)], 5: [(2, 2), (2, 3)]}
CASTS = {1: 0, 4: 1, 6: 2}
QCAST_SLOT = 2
MAX_SLOT = 11
DEN_SLOT, OUT_SLOT = 1, 2


def pair_at(j):
    q, g = j // 6, j % 6
    return GROUP_AT[g] + q * PAIR_Q


def positions():
    return sorted(range(PAIRS), key=pair_at)


def build(nc, x, ctx, mask, wq, wout, gamma, beta, out):
    with ExitStack() as stack:
        def sb(name, shape, dt=F32):
            return stack.enter_context(nc.sbuf_tensor(name, shape, dt))

        def sem(name):
            return stack.enter_context(nc.semaphore(name))

        q_all = nc.dram_tensor("q_all", [HIDDEN, BATCH * QUERIES], F32, kind="Internal").ap()
        key_rows = nc.dram_tensor("key_rows", [BATCH, 2, SLOTS * 128], F32, kind="Internal").ap()

        kT = sb("kT", [128, 2, CHUNKS, GROUPS, CHUNK, 128])
        kTb = sb("kTb", [128, 2, GROUPS, CHUNK, 128], BF16)
        k_src = sb("k_src", [128, 2, BLOCKS, CHUNK, GROUPS * PAIR])
        v = sb("v", [128, CHUNKS, CHUNK, HIDDEN])
        probs = sb("probs", [128, 3, ALL_Q])
        prob_sum = sb("prob_sum", [128, ALL_Q])
        qd = sb("qd", [128, 2, ALL_Q])
        qdb = sb("qdb", [128, ALL_Q], BF16)
        woutT = sb("woutT", [128, KC, HIDDEN])
        ident = sb("ident", [128, 128])
        ones = sb("ones", [128, 64])
        block_of = sb("block_of", [128, 8])
        own_head = sb("own_head", [128, 4])
        tile_max = sb("tile_max", [128, CHUNKS, PAIRS])
        neg_max = sb("neg_max", [128, PAIRS])
        neg_maxT = sb("neg_maxT", [16, PAIR_Q])
        head_sel = sb("head_sel", [128, KC, QUERIES])
        den_sel = sb("den_sel", [128, KC, QUERIES])
        den_inv = sb("den_inv", [128, KC, QUERIES])
        attnT = sb("attnT", [128, KC, PAIR_Q])
        x_res = sb("x_res", [128, HIDDEN])
        result = sb("result", [128, HIDDEN])
        stats = sb("stats", [128, TQ, TQ_TILES, 6])
        mean_var = sb("mean_var", [128, TQ, TQ_TILES, 2])
        rstd = sb("rstd", [128, TQ, TQ_TILES])
        ln_weights = sb("ln_weights", [128, 2, KC])
        mask_u8 = sb("mask_u8", [BATCH, CONTEXT], mybir.dt.uint8)

        kT1 = kT[:, 1].rearrange("p c g k m -> p (c g k m)")
        x_size, xT_size, w_size = TQ_TILES * HIDDEN, KC * TQ_COLS, KC * HIDDEN
        x_in = kT1[:, 0:2 * x_size].rearrange("p (r i n) -> p r i n", r=2, i=TQ_TILES)
        xT = kT1[:, 2 * x_size:2 * x_size + 2 * xT_size].rearrange("p (r c n) -> p r c n", r=2, c=KC)
        p_flat = probs[:].rearrange("p r n -> p (r n)")
        wq_nat = p_flat[:, 0:w_size].rearrange("p (c n) -> p c n", c=KC)
        wqT = p_flat[:, w_size:2 * w_size].rearrange("p (c n) -> p c n", c=KC)
        wout_nat = v[:, 1]
        qT_out = v[:, 2].rearrange("p k n -> p (k n)")[:, 0:KC * TQ_COLS].rearrange("p (c n) -> p c n", c=KC)
        mask_rows = prob_sum[0:BATCH, 0:SLOTS * 128].rearrange("p (k m) -> p k m", k=SLOTS)
        one_rows = v[0:BATCH, 0].rearrange("p k n -> p (k n)")[:, 0:SLOTS * 128]

        ps = stack.enter_context(nc.psum_tensor("ps", [128, 8, 512], F32))
        score_banks = [ps[:, 0:2, :], ps[:, 2:4, :]]
        head_acc = ps[:, 4:6, :].rearrange("p b n -> p (b n)").rearrange("p (r n) -> p r n", r=KC)
        den_acc = ps[:, 6:8, :].rearrange("p b n -> p (b n)").rearrange("p (r n) -> p r n", r=KC)
        aux = [ps[:, 6, :], ps[:, 7, :]]

        x_landed = [sem(f"x_landed{i}") for i in range(TQ)]
        w_landed = [sem("wq_landed"), sem("wout_landed")]
        ln_landed = sem("ln_landed")
        mask_landed = sem("mask_landed")
        rows_ready = sem("rows_ready")
        rows_stored = sem("rows_stored")
        zeroed = sem("zeroed")
        consts = sem("consts")
        stats_steps = sem("stats_steps")
        rstd_ready = sem("rstd_ready")
        var_ready = sem("var_ready")
        std_ready = sem("std_ready")
        x_normed = sem("x_normed")
        pro_filled = sem("pro_filled")
        pro_drained = sem("pro_drained")
        q_stored = [sem(f"q_stored{i}") for i in range(TQ)]
        src_landed = [sem("src_landed0"), sem("src_landed1")]
        kT_turned = sem("kT_turned")
        rows_landed = [sem("rows_landed0"), sem("rows_landed1")]
        v_landed = [sem(f"v_landed{c}") for c in range(CHUNKS)]
        q_landed = [sem("q_landed0"), sem("q_landed1")]
        qdb_cast = sem("qdb_cast")
        kTb_cast = sem("kTb_cast")
        tile_scored = sem("tile_scored")
        tile_taken = sem("tile_taken")
        max_ready = sem("max_ready")
        max_turned = sem("max_turned")
        max_copied = sem("max_copied")
        max_landed = sem("max_landed")
        unit_scored = sem("unit_scored")
        unit_exped = sem("unit_exped")
        pv_done = sem("pv_done")
        summed = sem("summed")
        den_scored = sem("den_scored")
        den_taken = sem("den_taken")
        heads_taken = sem("heads_taken")
        own_steps = sem("own_steps")
        attn_ready = sem("attn_ready")
        projected = sem("projected")
        res_landed = sem("res_landed")
        result_ready = sem("result_ready")
        result_stored = sem("result_stored")

        OWN = 7

        def nth(per, bt, extra):
            return bt[0] * (2 * per) + (per * bt[1] + extra)

        def nonzero(count):
            return not isinstance(count, int) or count > 0

        def after(bt, n):
            return (bt[0], bt[1] + n)

        def row0(ap2, bt, size):
            return ap2[bass.ds(bt[0] * 2 + bt[1], size)]

        def load_k_src(sp, bt, c):
            n = 3 * bt[1] + c
            rows = row0(ctx, bt, 1)[0, CHUNK * LANES * c:CHUNK * LANES * (c + 1), :]
            full = rows[0:TAIL * BLOCKS * CHUNK, :].rearrange("(r w) n -> r w n", r=TAIL)
            for q in range(3):
                w = QUAD_PAIRS[q] * PAIR
                cols = slice(GROUPS * PAIR * q, GROUPS * PAIR * q + w)
                dst = k_src[32 * q:32 * q + 32, n % 2].rearrange("p b k n -> p (b k) n")
                for lo, hi in ((0, 16), (16, TAIL)):
                    sp.dma_start(dst[lo:hi, :, 0:w], full[lo:hi, :, cols]).then_inc(src_landed[n % 2], 16)
                sp.dma_start(dst[TAIL:TAIL + 1, 0:CHUNK, 0:w], rows[TAIL * BLOCKS * CHUNK:, cols].unsqueeze(0)
                             ).then_inc(src_landed[n % 2], 16)
        SRC_DMAS = 3 * 3

        def load_v(sp, bt, c):
            rows = row0(ctx, bt, 1)[0, CHUNK * LANES * c:CHUNK * LANES * (c + 1), :]
            src = rows.rearrange("(m k) n -> m k n", k=CHUNK)
            for lo, hi in ((112, LANES), (0, 112)):
                sp.dma_start(v[lo:hi, c], src[lo:hi]).then_inc(v_landed[c], 16)

        def load_rows(sp, bt):
            src = row0(key_rows, bt, 1).rearrange("a r (c n) -> (a r) c n", c=CHUNKS)
            for c in range(CHUNKS):
                dst = kT[MAX_ROW:ROWS, bt[1] % 2, c].rearrange("p g k m -> p g (k m)")
                sp.dma_start(dst, src[:, c:c + 1, :].broadcast_to([2, GROUPS, CHUNK * 128])
                             ).then_inc(rows_landed[bt[1] % 2], 16)
        ROW_DMAS = CHUNKS

        def load_q(sp, bt):
            p = bt[1] % 2
            src = q_all.rearrange("(j e d) s -> e d j s", e=2, d=HEAD_DIM)
            here = bass.ds(bt[0] * (2 * QUERIES) + bt[1] * QUERIES, QUERIES)
            for q in range(3):
                for e in range(2):
                    r0, at = 32 * q + HEAD_DIM * e, q * PAIR_Q + e * QUERIES
                    for g0, g1 in ((0, 4), (4, 6)):
                        if g0 >= QUAD_PAIRS[q]:
                            continue
                        w = GROUP_PAIRS[g0] * PAIR_Q
                        dst = qd[r0:r0 + HEAD_DIM, p, GROUP_AT[g0]:GROUP_AT[g0] + (g1 - g0) * w]
                        dst = dst.rearrange("p (g n) -> p g n", g=g1 - g0)[:, :, at:at + QUERIES]
                        sp.dma_start(dst, src[e][:, 6 * q + g0:6 * q + g1, here]).then_inc(q_landed[p], 16)
        Q_DMAS = 2 * (2 + 2 + 1)

        def load_max(sp, bt):
            sp.wait_ge(max_copied, nth(1, bt, 1))
            sp.dma_start(qd[MAX_ROW:MAX_ROW + 1, bt[1] % 2].rearrange("p (j n) -> p j n", j=PAIRS),
                         neg_maxT[:, :]).then_inc(max_landed, 16)

        def turn(dve, bt, c, k):
            n = 3 * bt[1] + c
            if k == 0:
                dve.wait_ge(src_landed[n % 2], bt[0] * (3 * 16 * SRC_DMAS) + 16 * SRC_DMAS * (n // 2 + 1))
                free = nth(UNITS * SLOTS, bt, UNITS * (CHUNK * (c + 1) - 2 * SLOTS))
                if nonzero(free):
                    dve.wait_ge(unit_scored, free)
            src = k_src[0:KEY_ROWS, n % 2, :, k, :].rearrange("p b (g n) -> p g b n", g=GROUPS)
            dst = kT[0:KEY_ROWS, bt[1] % 2, c, :, k, :].rearrange("p g (r b) -> p g b r", b=BLOCKS)
            ins = nc.vector.transpose(dst, src)
            if k == CHUNK - 1:
                ins.then_inc(kT_turned, 1)

        def cast_q(act, bt):
            act.wait_ge(q_landed[bt[1] % 2], bt[0] * (16 * Q_DMAS) + 16 * Q_DMAS * (bt[1] // 2 + 1))
            used = nth(TILES, bt, 0)
            if nonzero(used):
                act.wait_ge(tile_scored, used)
            nc.scalar.copy(qdb[0:KEY_ROWS, :], qd[0:KEY_ROWS, bt[1] % 2, :]).then_inc(qdb_cast, 1)

        def cast_k(act, bt, c, half):
            n = 3 * bt[1] + c
            if half == 0:
                act.wait_ge(kT_turned, nth(CHUNKS, bt, c + 1))
                act.wait_ge(rows_landed[bt[1] % 2], bt[0] * (16 * ROW_DMAS) + 16 * ROW_DMAS * (bt[1] // 2 + 1))
                used = nth(TILES, bt, PAIRS * (c - 1))
                if nonzero(used):
                    act.wait_ge(tile_scored, used)
            gs = slice(3 * half, 3 * half + 3)
            ins = nc.scalar.copy(kTb[0:ROWS, n % 2, gs], kT[0:ROWS, bt[1] % 2, c, gs])
            if half == 1:
                ins.then_inc(kTb_cast, 1)

        def score_tile(pe, bt, i):
            c, at = i // PAIRS, i % PAIRS
            if i == 0:
                pe.wait_ge(qdb_cast, nth(1, bt, 1))
                for s, value in ((den_taken, nth(1, bt, -1)), (max_copied, nth(1, bt, 0))):
                    if nonzero(value):
                        pe.wait_ge(s, value)
                if bt[1] % 2 == 1:
                    if nonzero(bt[0]):
                        pe.wait_ge(result_ready, bt[0])
            if at == 0:
                pe.wait_ge(kTb_cast, nth(CHUNKS, bt, c + 1))
            free = nth(TILES, bt, i - 1)
            if nonzero(free):
                pe.wait_ge(tile_taken, free)
            g = positions()[at] % 6
            n = 3 * bt[1] + c
            nc.tensor.matmul(aux[i % 2][0:PAIR_Q, 0:CHUNK * LANES], qdb[0:ROWS, at * PAIR_Q:(at + 1) * PAIR_Q],
                             kTb[0:ROWS, n % 2, g, :, 0:LANES], start=True, stop=True).then_inc(tile_scored, 1)

        def take_tile(dve, bt, i):
            dve.wait_ge(tile_scored, nth(TILES, bt, i + 1))
            nc.vector.tensor_reduce(tile_max[0:PAIR_Q, i // PAIRS, i % PAIRS:i % PAIRS + 1],
                                    aux[i % 2][0:PAIR_Q, 0:CHUNK * LANES], AX_X, ALU.max).then_inc(tile_taken, 1)

        def take_max(dve, bt):
            dve.wait_ge(tile_taken, nth(TILES, bt, TILES))
            if nonzero(nth(1, bt, 0)):
                dve.wait_ge(max_turned, nth(1, bt, 0))
            nc.vector.tensor_reduce(neg_max[0:PAIR_Q, :], tile_max[0:PAIR_Q].rearrange("p c j -> p j c"),
                                    AX_X, ALU.max, negate=True).then_inc(max_ready, 1)

        def turn_max(pe, bt):
            pe.wait_ge(max_ready, nth(1, bt, 1))
            nc.tensor.transpose(aux[0][0:PAIRS, 0:PAIR_Q], neg_max[0:PAIR_Q, :],
                                ident[0:PAIR_Q, 0:PAIR_Q]).then_inc(max_turned, 1)

        def copy_max(act, bt):
            act.wait_ge(max_turned, nth(1, bt, 1))
            if nonzero(nth(16, bt, 0)):
                act.wait_ge(max_landed, nth(16, bt, 0))
            nc.scalar.copy(neg_maxT[:, :], aux[0][0:PAIRS, 0:PAIR_Q]).then_inc(max_copied, 1)

        def score_group(pe, bt, k, g):
            p, c = bt[1] % 2, k // CHUNK
            unit = UNITS * k + g // 2
            if k == 0 and g == 0:
                pe.wait_ge(max_landed, nth(16, bt, 16))
            if k % CHUNK == 0 and g == 0:
                pe.wait_ge(kT_turned, nth(CHUNKS, bt, c + 1))
            free = nth(UNITS * SLOTS, bt, unit - 1)
            if g % 2 == 0 and nonzero(free):
                pe.wait_ge(unit_exped, free)
            w = GROUP_PAIRS[g] * PAIR_Q
            mm = nc.tensor.matmul(score_banks[unit % 2][0:LANES, g % 2, 0:w],
                                  kT[0:ROWS, p, c, g, k % CHUNK, 0:LANES],
                                  qd[0:ROWS, p, GROUP_AT[g]:GROUP_AT[g] + w], start=True, stop=True)
            if g % 2 == 1:
                mm.then_inc(unit_scored, 1)

        def exp_unit(act, bt, k, u):
            unit = UNITS * k + u
            if u == 0:
                if nonzero(nth(SLOTS, bt, k - 2)):
                    act.wait_ge(pv_done, nth(SLOTS, bt, k - 2))
                used = nth(SLOTS - 1, bt, max(k - 3, 1) if k >= 3 else k - 2)
                if nonzero(used):
                    act.wait_ge(summed, used)
            act.wait_ge(unit_scored, nth(UNITS * SLOTS, bt, unit + 1))
            w = GROUP_PAIRS[2 * u] * PAIR_Q
            at = GROUP_AT[2 * u]
            nc.scalar.activation(probs[0:LANES, k % 3, at:at + 2 * w].rearrange("p (b n) -> p b n", b=2),
                                 score_banks[unit % 2][0:LANES, :, 0:w], ACT.Exp, scale=SCALE
                                 ).then_inc(unit_exped, 1)

        def pv_part(pe, bt, k, part):
            c = k // CHUNK
            if part == 0:
                pe.wait_ge(unit_exped, nth(UNITS * SLOTS, bt, UNITS * (k + 1)))
                if k % CHUNK == 0:
                    pe.wait_ge(v_landed[c], nth(32, bt, 32))
                if k == 0 and nonzero(nth(1, bt, 0)):
                    pe.wait_ge(heads_taken, nth(1, bt, 0))
            for u in (2 * part, 2 * part + 1):
                lo = 64 * (u % 2)
                mm = nc.tensor.matmul(head_acc[lo:lo + 64, u // 2, 0:QUAD_Q],
                                      v[0:LANES, c, k % CHUNK, 64 * u:64 * u + 64],
                                      quad(probs, k % 3, u), start=(k == 0 and (u // 2) % 2 == 0),
                                      stop=(k == SLOTS - 1), skip_group_check=True)
            if part == 3:
                mm.then_inc(pv_done, 1)

        def quad(tile, r, u):
            a, b = pair_at(2 * u), pair_at(2 * u + 1)
            step = b - a
            flat = tile[0:LANES].rearrange("p r n -> p (r n)") if r is not None else tile[0:LANES, :]
            at = a + (ALL_Q * r if r is not None else 0)
            two = flat[:, at:at + step + PAIR_Q]
            return bass.AP(two.tensor, two.offset, [list(two.ap[0]), [step, 2], [1, PAIR_Q]])

        def add_probs(pool, bt, k):
            pool.wait_ge(unit_exped, nth(UNITS * SLOTS, bt, UNITS * (k + 1)))
            if k == 1:
                if nonzero(nth(1, bt, 0)):
                    pool.wait_ge(den_scored, nth(1, bt, 0))
            else:
                pool.wait_ge(summed, nth(SLOTS - 1, bt, k - 1))
            first = probs[0:LANES, 0, :] if k == 1 else prob_sum[0:LANES, :]
            nc.gpsimd.tensor_tensor(prob_sum[0:LANES, :], first, probs[0:LANES, k % 3, :],
                                    ALU.add).then_inc(summed, 1)

        def score_den(pe, bt):
            pe.wait_ge(summed, nth(SLOTS - 1, bt, SLOTS - 1))
            if not (isinstance(bt[0], int) and nth(1, bt, 1) == BATCH):
                pe.wait_ge(max_copied, nth(1, bt, 2))
            if nonzero(nth(1, bt, 0)):
                pe.wait_ge(den_taken, nth(1, bt, 0))
            double = bt[0] + bt[1] // 2
            if bt[1] % 2 == 1 and nonzero(double):
                pe.wait_ge(result_ready, double)
            for u in range(QUADS):
                lo = 64 * (u % 2)
                mm = nc.tensor.matmul(den_acc[lo:lo + 64, u // 2, 0:QUAD_Q], ones[0:LANES, :],
                                      quad(prob_sum, None, u), start=True, stop=True)
            mm.then_inc(den_scored, 1)

        def own_heads(dve, acc, dst, first_step, done):
            for e in range(4):
                src = acc[:, :, QUERIES * e:QUERIES * (e + 1)]
                if e == 0:
                    nc.vector.tensor_scalar(dst[:], src, own_head[:, 0:1], None, ALU.mult).then_inc(own_steps, 1)
                    continue
                dve.wait_ge(own_steps, first_step + e - 1)
                ins = nc.vector.scalar_tensor_tensor(dst[:], src, own_head[:, e:e + 1], dst[:], ALU.mult, ALU.add)
                ins.then_inc(own_steps if e < 3 else done, 1)

        def finish_heads(dve, bt):
            if nonzero(nth(1, bt, 0)):
                dve.wait_ge(attn_ready, nth(1, bt, 0))
            dve.wait_ge(pv_done, nth(SLOTS, bt, SLOTS))
            own_heads(dve, head_acc, head_sel, nth(OWN, bt, 1), heads_taken)
            dve.wait_ge(den_scored, nth(1, bt, 1))
            own_heads(dve, den_acc, den_sel, nth(OWN, bt, 4), den_taken)
            dve.wait_ge(den_taken, nth(1, bt, 1))
            nc.vector.reciprocal(den_inv[:], den_sel[:]).then_inc(own_steps, 1)
            dve.wait_ge(own_steps, nth(OWN, bt, OWN))
            dve.wait_ge(heads_taken, nth(1, bt, 1))
            if bt[1] % 2 == 0 and nonzero(bt[0] + bt[1] // 2):
                dve.wait_ge(projected, bt[0] + bt[1] // 2)
            at = QUERIES * (bt[1] % 2)
            nc.vector.tensor_tensor(attnT[:, :, at:at + QUERIES], head_sel[:], den_inv[:],
                                    ALU.mult).then_inc(attn_ready, 1)

        def project_out(pe, bt):
            pe.wait_ge(attn_ready, nth(1, bt, 1))
            pe.wait_ge(den_taken, nth(1, bt, 1))
            for c in range(KC):
                mm = nc.tensor.matmul(aux[0][0:PAIR_Q, :], attnT[:, c, :], woutT[:, c, :],
                                      start=(c == 0), stop=(c == KC - 1))
            mm.then_inc(projected, 1)

        def add_residual(dve, i):
            dve.wait_ge(projected, i + 1)
            dve.wait_ge(res_landed, i * 16 + 16)
            if nonzero(i):
                dve.wait_ge(result_stored, i * 16)
            nc.vector.tensor_tensor(result[0:PAIR_Q, :], aux[0][0:PAIR_Q, :], x_res[0:PAIR_Q, :],
                                    ALU.add).then_inc(result_ready, 1)

        x_rows = x.rearrange("(i b) s n -> i (b s) n", b=2)
        out_rows = out.rearrange("(i b) s n -> i (b s) n", b=2)

        def load_residual(sp, i):
            if nonzero(i):
                sp.wait_ge(result_ready, i)
            sp.dma_start(x_res[0:PAIR_Q, :], x_rows[bass.ds(i, 1)].rearrange("a p n -> (a p) n")
                         ).then_inc(res_landed, 16)

        def store_result(sp, i):
            sp.wait_ge(result_ready, i + 1)
            sp.dma_start(out_rows[bass.ds(i, 1)].rearrange("a p n -> (a p) n"), result[0:PAIR_Q, :]
                         ).then_inc(result_stored, 16)

        def loop(eng, body):
            body(0, first=True, last=False)
            with eng.Fori(1, BATCH // 2 - 1) as i:
                body(i, first=False, last=False)
            body(BATCH // 2 - 1, first=False, last=True)

        block = stack.enter_context(nc.Block())

        @block.sync
        def _(sp):
            def load_x(i):
                src = x_rows.rearrange("i p n -> p i n")[:, TQ_TILES * i:TQ_TILES * (i + 1)]
                sp.dma_start(x_in[0:PAIR_Q, i % 2], src).then_inc(x_landed[i], 16)

            def store_q(i):
                for c in range(KC):
                    if i == TQ - 1 and c == KC - 1:
                        load_max(sp, b0)
                    sp.wait_ge(pro_drained, filled_at("q", i, c) + 1)
                    sp.dma_start(q_all[128 * c:128 * (c + 1), TQ_COLS * i:TQ_COLS * (i + 1)],
                                 qT_out[:, c, :]).then_inc(q_stored[i], 16)

            b0 = (0, 0)
            load_x(0)
            sp.dma_start(wq_nat, wq.rearrange("(c p) n -> p c n", p=128)).then_inc(w_landed[0], 16)
            sp.dma_start(mask_u8[:, :], mask).then_inc(mask_landed, 16)
            load_x(1)
            for n, weight in enumerate((gamma, beta)):
                sp.dma_start(ln_weights[:, n, :], weight.rearrange("(c p) -> p c", p=128),
                             allow_slow_non_contiguous=True).then_inc(ln_landed, 16)
            sp.dma_start(wout_nat, wout.rearrange("(c p) n -> p c n", p=128)).then_inc(w_landed[1], 16)
            sp.wait_ge(zeroed, 1)
            load_k_src(sp, b0, 0)
            sp.wait_ge(rows_ready, 1)
            sp.wait_ge(consts, ROWS_SET)
            sp.dma_start(key_rows[:, 1, :], mask_rows.rearrange("p k m -> p (k m)")).then_inc(rows_stored, 16)
            sp.dma_start(key_rows[:, 0, :], one_rows).then_inc(rows_stored, 16)
            sp.wait_ge(zeroed, 2)
            load_k_src(sp, b0, 1)
            sp.wait_ge(rows_stored, 32)
            load_rows(sp, b0)
            load_v(sp, b0, 0)
            sp.wait_ge(pro_filled, filled_at("xT", 0, KC - 1) + 1)
            load_x(2)
            sp.wait_ge(kT_turned, 1)
            load_k_src(sp, b0, 2)
            store_q(0)
            sp.wait_ge(pro_filled, filled_at("xT", 1, KC - 1) + 1)
            load_x(3)
            sp.wait_ge(q_stored[0], 16 * KC)
            sp.wait_ge(consts, CONSTS)
            load_q(sp, b0)
            sp.wait_ge(pro_filled, filled_at("wout", KC - 1, 0) + 1)
            load_v(sp, b0, 1)
            load_q(sp, (0, 1))
            store_q(1)
            sp.wait_ge(kT_turned, 2)
            load_k_src(sp, (0, 1), 0)
            store_q(2)
            sp.wait_ge(kT_turned, 3)
            load_k_src(sp, (0, 1), 1)
            store_q(3)
            for i in range(1, TQ):
                sp.wait_ge(q_stored[i], 16 * KC)
            load_v(sp, b0, 2)
            sp.wait_ge(pro_filled, PRO_UNITS)

            def body(i, first, last):
                for o in range(2):
                    bt, nxt = (i, o), (i, o + 1)
                    final = last and o == 1
                    if not (first and o == 0):
                        sp.wait_ge(unit_scored, nth(UNITS * SLOTS, bt, 0))
                    if not final:
                        if not (first and o == 0):
                            load_q(sp, nxt)
                        load_rows(sp, nxt)
                    if not (first and o == 0):
                        sp.wait_ge(pv_done, nth(SLOTS, bt, 0))
                        load_v(sp, bt, 2)
                    if o == 1:
                        load_residual(sp, i)
                    if not final:
                        sp.wait_ge(kT_turned, nth(CHUNKS, nxt, 1))
                        load_k_src(sp, nxt, 2)
                    if o == 0 and not first:
                        store_result(sp, i - 1)
                    if not last:
                        sp.wait_ge(kT_turned, nth(CHUNKS, nxt, 2))
                        load_k_src(sp, after(nxt, 1), 0)
                    if not final:
                        sp.wait_ge(pv_done, nth(SLOTS, bt, CHUNK))
                        load_v(sp, nxt, 0)
                    if not last:
                        sp.wait_ge(kT_turned, nth(CHUNKS, nxt, 3))
                        load_k_src(sp, after(nxt, 1), 1)
                    if not final:
                        sp.wait_ge(pv_done, nth(SLOTS, bt, 2 * CHUNK))
                        load_v(sp, nxt, 1)
                        load_max(sp, nxt)

            loop(sp, body)
            store_result(sp, BATCH // 2 - 1)
            sp.wait_ge(result_stored, 16 * (BATCH // 2))

        @block.gpsimd
        def _(pool):
            nc.gpsimd.memset(ident[:], 0.0).then_inc(consts, 1)
            pool.wait_ge(consts, 1)
            nc.gpsimd.affine_select(out=ident[:], in_=ident[:], compare_op=ALU.not_equal, fill=1.0, base=0,
                                    pattern=[[-1, 128]], channel_multiplier=1).then_inc(consts, 1)
            pool.wait_ge(consts, IDENT)
            nc.gpsimd.memset(mask_rows[:, :, LANES:128], 0.0).then_inc(consts, 1)
            pool.wait_ge(consts, 3)
            nc.gpsimd.memset(one_rows, 1.0).then_inc(consts, 1)
            pool.wait_ge(consts, ROWS_SET)
            nc.gpsimd.memset(qd[0:KEY_ROWS], 0.0).then_inc(consts, 1)
            pool.wait_ge(consts, 5)
            nc.gpsimd.memset(qd[MAX_ROW:ROWS], 2.0).then_inc(consts, 1)
            pool.wait_ge(consts, 6)
            nc.gpsimd.memset(qdb[MAX_ROW:ROWS, :], 1.0).then_inc(consts, 1)
            pool.wait_ge(consts, 7)
            nc.gpsimd.memset(qdb[MAX_ROW:MAX_ROW + 1, :], 0.0).then_inc(consts, 1)
            pool.wait_ge(consts, 8)
            nc.gpsimd.memset(ones[:], 1.0).then_inc(consts, 1)
            pool.wait_ge(consts, 9)
            nc.gpsimd.memset(block_of[:], 1.0).then_inc(consts, 1)
            pool.wait_ge(consts, 10)
            nc.gpsimd.affine_select(out=block_of[:], in_=block_of[:], compare_op=ALU.is_ge, fill=0.0, base=0,
                                    pattern=[[-HEAD_DIM, 8]], channel_multiplier=1).then_inc(consts, 1)
            pool.wait_ge(consts, 11)
            nc.gpsimd.affine_select(out=block_of[:], in_=block_of[:], compare_op=ALU.is_ge, fill=0.0,
                                    base=HEAD_DIM - 1, pattern=[[HEAD_DIM, 8]],
                                    channel_multiplier=-1).then_inc(consts, 1)
            pool.wait_ge(consts, 12)
            nc.gpsimd.tensor_tensor(own_head[:], block_of[:, 0:4], block_of[:, 4:8], ALU.add).then_inc(consts, 1)
            pool.wait_ge(consts, CONSTS)

            def body(i, first, last):
                for o in range(2):
                    for k in range(1, SLOTS):
                        add_probs(pool, (i, o), k)

            loop(pool, body)

        @block.vector
        def _(dve):
            def statistics(i):
                dve.wait_ge(x_landed[i], 16)
                for t in range(TQ_TILES):
                    ins = nc.vector.bn_stats(stats[0:PAIR_Q, i, t, :], x_in[0:PAIR_Q, i % 2, t, :])
                ins.then_inc(stats_steps, 1)
                dve.wait_ge(stats_steps, 2 * i + 1)
                for t in range(TQ_TILES):
                    ins = nc.vector.bn_aggr(mean_var[0:PAIR_Q, i, t, :], stats[0:PAIR_Q, i, t, :])
                ins.then_inc(stats_steps, 1)
                dve.wait_ge(stats_steps, 2 * i + 2)
                nc.vector.tensor_scalar(rstd[0:PAIR_Q, i], mean_var[0:PAIR_Q, i, :, 1], LN_EPS, None,
                                        ALU.add).then_inc(var_ready, 1)

            def normalise(i):
                dve.wait_ge(std_ready, i + 1)
                nc.vector.reciprocal(rstd[0:PAIR_Q, i], rstd[0:PAIR_Q, i]).then_inc(rstd_ready, 1)
                dve.wait_ge(rstd_ready, i + 1)
                for t in range(TQ_TILES):
                    ins = nc.vector.tensor_scalar(x_in[0:PAIR_Q, i % 2, t, :], x_in[0:PAIR_Q, i % 2, t, :],
                                                  mean_var[0:PAIR_Q, i, t, 0:1], rstd[0:PAIR_Q, i, t:t + 1],
                                                  ALU.subtract, ALU.mult)
                ins.then_inc(x_normed, 1)

            b0 = (0, 0)
            nc.vector.memset(k_src[0:KEY_ROWS, 0], 0.0).then_inc(zeroed, 1)
            statistics(0)
            normalise(0)
            nc.vector.memset(k_src[0:KEY_ROWS, 1], 0.0).then_inc(zeroed, 1)
            dve.wait_ge(mask_landed, 16)
            mask_in = mask_u8[:, :].rearrange("p (c m k) -> p c k m", c=CHUNKS, k=CHUNK)
            nc.vector.tensor_scalar(mask_rows[:, :, 0:LANES].rearrange("p (c k) m -> p c k m", c=CHUNKS), mask_in,
                                    MASKED, -MASKED, ALU.mult, ALU.add).then_inc(rows_ready, 1)
            statistics(1)
            normalise(1)
            for k in range(CHUNK):
                turn(dve, b0, 0, k)
            for k in range(CHUNK):
                turn(dve, b0, 1, k)
            statistics(2)
            for k in range(CHUNK):
                turn(dve, b0, 2, k)
            normalise(2)
            statistics(3)
            normalise(3)
            for t in range(TILES):
                take_tile(dve, b0, t)
            take_max(dve, b0)
            dve.wait_ge(pro_filled, PRO_UNITS)

            def body(i, first, last):
                for o in range(2):
                    bt, nxt = (i, o), (i, o + 1)
                    final = last and o == 1
                    for k in range(SLOTS):
                        if k == DEN_SLOT and not (first and o == 0):
                            finish_heads(dve, after(bt, -1))
                        turns = list(TURNS.get(k, [])) if not final else []
                        at = (k - FIRST_TILE_SLOT) * TILES_PER_SLOT
                        if 0 <= at < TILES and not final:
                            for t in range(at, at + TILES_PER_SLOT):
                                take_tile(dve, nxt, t)
                                if t % 3 == 1 and turns:
                                    turn(dve, nxt, *turns.pop(0))
                        for c, kk in turns:
                            turn(dve, nxt, c, kk)
                        if k == OUT_SLOT and o == 0 and not first:
                            add_residual(dve, i - 1)
                        if k == MAX_SLOT - 1 and not final:
                            take_max(dve, nxt)

            loop(dve, body)
            finish_heads(dve, (BATCH // 2 - 1, 1))
            add_residual(dve, BATCH // 2 - 1)

        @block.scalar
        def _(act):
            b0 = (0, 0)
            for kind, a, b in PRO_PLAN:
                if kind == "std":
                    act.wait_ge(var_ready, a + 1)
                    nc.scalar.activation(rstd[0:PAIR_Q, a], rstd[0:PAIR_Q, a], ACT.Sqrt).then_inc(std_ready, 1)
                    continue
                if kind == "cast_q":
                    act.wait_ge(consts, CONSTS)
                    cast_q(act, b0)
                    continue
                if kind == "cast_k":
                    cast_k(act, b0, a, 0)
                    cast_k(act, b0, a, 1)
                    continue
                if kind == "max":
                    copy_max(act, b0)
                    continue
                unit = filled_at(kind, a, b)
                act.wait_ge(pro_filled, unit + 1)
                src = ps[:, pro_bank(unit), :]
                if kind == "wq":
                    nc.scalar.copy(wqT[:, a, :], src).then_inc(pro_drained, 1)
                elif kind == "wout":
                    nc.scalar.copy(woutT[:, a, :], src).then_inc(pro_drained, 1)
                elif kind == "xT":
                    if b == 0:
                        act.wait_ge(ln_landed, 32)
                    nc.scalar.activation(xT[:, a % 2, b, :], src[:, 0:TQ_COLS], ACT.Identity,
                                         bias=ln_weights[:, 1, b:b + 1],
                                         scale=ln_weights[:, 0, b:b + 1]).then_inc(pro_drained, 1)
                else:
                    if a >= 1:
                        act.wait_ge(q_stored[a - 1], 16 * KC)
                    nc.scalar.copy(qT_out[:, b, :], src[:, 0:TQ_COLS]).then_inc(pro_drained, 1)

            def body(i, first, last):
                for o in range(2):
                    bt, nxt = (i, o), (i, o + 1)
                    final = last and o == 1
                    for k in range(SLOTS):
                        exp_unit(act, bt, k, 0)
                        if k == QCAST_SLOT and not final:
                            cast_q(act, nxt)
                        if k == MAX_SLOT and not final:
                            copy_max(act, nxt)
                        exp_unit(act, bt, k, 1)
                        if k in CASTS and not final:
                            cast_k(act, nxt, CASTS[k], 0)
                        exp_unit(act, bt, k, 2)
                        if k in CASTS and not final:
                            cast_k(act, nxt, CASTS[k], 1)

            loop(act, body)

        @block.tensor
        def _(pe):
            b0 = (0, 0)
            pe.wait_ge(consts, IDENT)
            for kind, a, b in PRO_PLAN:
                if kind in PRO_NO_FILL:
                    continue
                unit = filled_at(kind, a, b)
                if unit >= PRO_BANKS:
                    pe.wait_ge(pro_drained, unit - PRO_BANKS + 1)
                bank = ps[:, pro_bank(unit), :]
                if kind in ("wq", "wout"):
                    w, landed = (wq_nat, w_landed[0]) if kind == "wq" else (wout_nat, w_landed[1])
                    pe.wait_ge(landed, 16)
                    for c in range(KC):
                        mm = nc.tensor.transpose(bank[:, 128 * c:128 * (c + 1)], w[:, c, 128 * a:128 * (a + 1)],
                                                 ident[:, :])
                elif kind == "xT":
                    pe.wait_ge(x_normed, a + 1)
                    for t in range(TQ_TILES):
                        mm = nc.tensor.transpose(bank[:, PAIR_Q * t:PAIR_Q * (t + 1)],
                                                 x_in[0:PAIR_Q, a % 2, t, 128 * b:128 * (b + 1)],
                                                 ident[0:PAIR_Q, 0:PAIR_Q])
                else:
                    if b == 0:
                        pe.wait_ge(pro_drained, filled_at("xT", a, KC - 1) + 1)
                    for c in range(KC):
                        mm = nc.tensor.matmul(bank[:, 0:TQ_COLS], wqT[:, c, 128 * b:128 * (b + 1)],
                                              xT[:, a % 2, c, :], start=(c == 0), stop=(c == KC - 1))
                        if c == KC - 1:
                            mm.then_inc(pro_filled, 1)
                        step = KC * KC * a + KC * b + c - FIRST_TILE_PRODUCT
                        for t in range(3 * step // 2, 3 * (step + 1) // 2):
                            if 0 <= t < TILES:
                                score_tile(pe, b0, t)
                        if step == 2 * TILES // 3 + 1:
                            turn_max(pe, b0)
                    continue
                mm.then_inc(pro_filled, 1)
            pe.wait_ge(pro_drained, PRO_UNITS - 2)

            def body(i, first, last):
                for o in range(2):
                    bt, nxt, prev = (i, o), (i, o + 1), (i, o - 1)
                    final = last and o == 1
                    for k in range(SLOTS):
                        at = (k - FIRST_TILE_SLOT) * TILES_PER_SLOT
                        tiles = list(range(at, at + TILES_PER_SLOT)) if 0 <= at < TILES and not final else []
                        pv = (bt, k - 1) if k > 0 else (prev, SLOTS - 1)
                        has_pv = k > 0 or not (first and o == 0)
                        order = TILE_ORDER if tiles else MAX_ORDER if k == MAX_SLOT and not final else PLAIN_ORDER
                        for what, n in order:
                            if what == "scores":
                                score_group(pe, bt, k, n)
                            elif what == "tile":
                                score_tile(pe, nxt, tiles[n])
                            elif what == "pv" and has_pv:
                                pv_part(pe, pv[0], pv[1], n)
                            elif what == "max":
                                turn_max(pe, nxt)
                            elif what == "finish" and k == DEN_SLOT and not (first and o == 0):
                                score_den(pe, prev)
                            elif what == "finish" and k == OUT_SLOT and o == 0 and not first:
                                project_out(pe, prev)

            loop(pe, body)
            end = (BATCH // 2 - 1, 1)
            for part in range(4):
                pv_part(pe, end, SLOTS - 1, part)
            score_den(pe, end)
            project_out(pe, end)


TILE_ORDER = [("scores", 0), ("tile", 0), ("scores", 1), ("pv", 0), ("tile", 1), ("scores", 2), ("pv", 1),
              ("tile", 2), ("scores", 3), ("pv", 2), ("tile", 3), ("scores", 4), ("tile", 4), ("scores", 5),
              ("pv", 3), ("tile", 5)]
PLAIN_ORDER = [("scores", 0), ("scores", 1), ("finish", 0), ("scores", 2), ("scores", 3), ("pv", 0), ("pv", 1),
               ("pv", 2), ("pv", 3), ("scores", 4), ("scores", 5)]
MAX_ORDER = [("scores", 0), ("scores", 1), ("pv", 0), ("max", 0), ("scores", 2), ("scores", 3), ("pv", 1),
             ("pv", 2), ("pv", 3), ("scores", 4), ("scores", 5)]


PRO_NO_FILL = ("std", "cast_q", "cast_k", "max")


def _plan():
    def columns(kind, a, cols=range(KC)):
        return [(kind, a, c) for c in cols]

    plan = [("std", 0, 0)] + [("wq", c, 0) for c in range(KC)] + columns("xT", 0) + [("std", 1, 0)]
    plan += columns("q", 0) + columns("xT", 1) + [("cast_k", 0, 0)] + [("wout", c, 0) for c in range(KC)]
    plan += [("std", 2, 0)] + columns("q", 1, (0,)) + [("cast_k", 1, 0)] + columns("q", 1, (1,))
    plan += [("std", 3, 0), ("cast_q", 0, 0)] + columns("q", 1, (2,)) + columns("xT", 2) + columns("q", 1, (3,))
    plan += columns("q", 2, (0, 1)) + [("cast_k", 2, 0)] + columns("q", 2, (2,)) + columns("xT", 3)
    plan += columns("q", 2, (3,)) + columns("q", 3, (0, 1, 2)) + [("max", 0, 0)] + columns("q", 3, (3,))
    return plan


PRO_PLAN = _plan()
PRO_FILLS = [p for p in PRO_PLAN if p[0] not in PRO_NO_FILL]
FIRST_TILE_PRODUCT = 2 * KC * KC - KC
PRO_UNITS = len(PRO_FILLS)
PRO_BANKS = 6
IDENT, ROWS_SET, CONSTS = 2, 4, 13


def pro_bank(unit):
    return (unit - PRO_UNITS) % PRO_BANKS


def filled_at(kind, a, b):
    return PRO_FILLS.index((kind, a, b))


_INS = ["x", "ctx_4096", "mask_BxS2_bf1", "L0_xattn_Wq", "L0_xattn_Wout", "L0_xattn_ln_gamma", "L0_xattn_ln_beta"]


def kernel(**inputs):
    import numpy as np
    import concourse.bacc as bacc
    from concourse.bass_utils import run_bass_kernel_spmd

    nc = bacc.Bacc("TRN2", target_bir_lowering=False, num_devices=1)
    arrays, args = {}, []
    for name in _INS:
        a = np.ascontiguousarray(inputs[name])
        if a.dtype == np.bool_:
            a = a.view(np.uint8)
        arrays[f"in_{name}"] = a
        args.append(nc.dram_tensor(f"in_{name}", a.shape, mybir.dt.from_np(a.dtype), kind="ExternalInput").ap())
    out = nc.dram_tensor("out", [BATCH, QUERIES, HIDDEN], F32, kind="ExternalOutput").ap()
    build(nc, *args, out)
    r = run_bass_kernel_spmd(nc, [arrays], core_ids=[0])
    return r.results[0]["out"]
```
